# Optimizing a Trainium2 kernel written in Bass

```python
import numpy as np
import jax
import jax.numpy as jnp

def _softmax(x, axis=-1):
    return jax.nn.softmax(x, axis=axis)

def _gelu(x):
    return jax.nn.gelu(x, approximate=True)

def _silu(x):
    return jax.nn.silu(x)

def _sigmoid(x):
    return jax.nn.sigmoid(x)

def _layernorm(x, axis=-1, eps=1e-05):
    m = jnp.mean(x, axis=axis, keepdims=True)
    v = jnp.var(x, axis=axis, keepdims=True)
    return (x - m) / jnp.sqrt(v + eps)

def _scatter_add(tgt, idx, src, axis=0):
    return tgt.at[idx].add(src)

def _segment_sum(src, seg, n):
    return jax.ops.segment_sum(src, seg, n)
kernel_name = 'mk_adj_resnorm_d1_adj_r2_d5b27e'

def setup_inputs(seed: int=0):
    np.random.seed(seed)
    _w = jnp.asarray

    def _rec_inputs():
        import jax
        import jax.numpy as jnp
        _gk = jax.random.key(seed)
        x = -0.0001538 + 1 * jax.random.normal(jax.random.fold_in(_gk, 1), (128, 128, 384), jnp.float32)
        _a = jax.random.bernoulli(jax.random.fold_in(_gk, 2), 0.03125, (128, 128, 128))
        _a = jnp.logical_or(_a, jnp.eye(128, dtype=bool))
        adj = _a
        return (x, adj)
    x, adj = _rec_inputs()

    def _L0_gnn_setup():
        import jax, jax.numpy as jnp
        import numpy as np
        B, S, H = (4, 1024, 384)
        NUM_HEADS = 6
        HEAD_SIZE = H // NUM_HEADS
        NEG = -9000000000000000.0

        def _heads(x):
            b, s, _ = x.shape
            return x.reshape(b, s, NUM_HEADS, HEAD_SIZE).transpose(0, 2, 1, 3)
        key = jax.random.key(seed)
        ks = jax.random.split(key, 10)
        seq_inputs = jax.random.normal(ks[0], (B, S, H), dtype=jnp.float32)
        gm = jax.random.randint(ks[1], (B, S, S), 0, 2) > 0
        graph_mask = gm | jnp.eye(S, dtype=bool)[None]
        sc = 1.0 / np.sqrt(H)
        Wq = jax.random.normal(ks[2], (H, H), dtype=jnp.float32) * sc
        bq = jnp.zeros((H,), dtype=jnp.float32)
        Wk = jax.random.normal(ks[3], (H, H), dtype=jnp.float32) * sc
        bk = jnp.zeros((H,), dtype=jnp.float32)
        Wv = jax.random.normal(ks[4], (H, H), dtype=jnp.float32) * sc
        bv = jnp.zeros((H,), dtype=jnp.float32)
        Wf = jax.random.normal(ks[5], (H, H), dtype=jnp.float32) * sc
        bf = jnp.zeros((H,), dtype=jnp.float32)
        return {'seq_inputs': seq_inputs, 'Wq': Wq, 'bq': bq, 'Wk': Wk, 'bk': bk, 'Wv': Wv, 'bv': bv, 'Wf': Wf, 'bf': bf, 'graph_mask': graph_mask}
    _L0_gnn_all = _L0_gnn_setup()
    _L0_gnn_in = {k: v for k, v in _L0_gnn_all.items() if k in ('Wq', 'bq', 'Wk', 'bk', 'Wv', 'bv', 'Wf', 'bf')}
    del _L0_gnn_all
    return {'x': x, 'adj': adj, 'L0_gnn_Wq': _L0_gnn_in['Wq'], 'L0_gnn_bq': _L0_gnn_in['bq'], 'L0_gnn_Wk': _L0_gnn_in['Wk'], 'L0_gnn_bk': _L0_gnn_in['bk'], 'L0_gnn_Wv': _L0_gnn_in['Wv'], 'L0_gnn_bv': _L0_gnn_in['bv'], 'L0_gnn_Wf': _L0_gnn_in['Wf'], 'L0_gnn_bf': _L0_gnn_in['bf']}

def reference(x, adj, L0_gnn_Wq, L0_gnn_bq, L0_gnn_Wk, L0_gnn_bk, L0_gnn_Wv, L0_gnn_bv, L0_gnn_Wf, L0_gnn_bf):
    import jax
    import jax.numpy as jnp

    def _L0_gnn_ref(seq_inputs, Wq, bq, Wk, bk, Wv, bv, Wf, bf, graph_mask):
        import jax, jax.numpy as jnp
        import numpy as np
        B, S, H = (4, 1024, 384)
        NUM_HEADS = 6
        HEAD_SIZE = H // NUM_HEADS
        NEG = -9000000000000000.0

        def _heads(x):
            b, s, _ = x.shape
            return x.reshape(b, s, NUM_HEADS, HEAD_SIZE).transpose(0, 2, 1, 3)
        q = _heads(seq_inputs @ Wq + bq)
        k = _heads(seq_inputs @ Wk + bk)
        v = _heads(seq_inputs @ Wv + bv)
        scores = jnp.einsum('bhqd,bhkd->bhqk', q, k) / np.sqrt(HEAD_SIZE)
        bias = jnp.where(graph_mask, 0.0, NEG)[:, None]
        probs = jax.nn.softmax(scores + bias, axis=-1)
        ctx = jnp.einsum('bhqk,bhkd->bhqd', probs, v)
        ctx = ctx.transpose(0, 2, 1, 3).reshape(seq_inputs.shape[0], seq_inputs.shape[1], H)
        return ctx @ Wf + bf
    x = _layernorm(x + _L0_gnn_ref(x, L0_gnn_Wq, L0_gnn_bq, L0_gnn_Wk, L0_gnn_bk, L0_gnn_Wv, L0_gnn_bv, L0_gnn_Wf, L0_gnn_bf, adj), axis=-1)
    return x

_drawn_inputs = setup_inputs


def setup_inputs(seed=0):
    import zlib

    import numpy as np

    out = dict(_drawn_inputs(seed))
    spreads = {'L0_gnn_bq': (0.0, 0.1),
     'L0_gnn_bk': (0.0, 0.1),
     'L0_gnn_bv': (0.0, 0.1),
     'L0_gnn_bf': (0.0, 0.1)}
    factors = {}
    for name, (base, spread) in spreads.items():
        noise = np.random.default_rng([zlib.crc32(name.encode()), seed]).standard_normal(out[name].shape)
        drawn = base * np.exp(spread * noise) if base else spread * noise
        out[name] = jnp.asarray(drawn.astype(out[name].dtype))
    for name, factor in factors.items():
        out[name] = (out[name] * factor).astype(out[name].dtype)
    return out
```

```python
from contextlib import ExitStack

import concourse.bass as bass
from concourse import mybir

ALU = mybir.AluOpType
ACT = mybir.ActivationFunctionType
AX = mybir.AxisListType
F32 = mybir.dt.float32
F32R = mybir.dt.float32r
U8 = mybir.dt.uint8

P = 128
BATCH = 128
SEQ = 128
HID = 384
HEADS = 6
HEAD = HID // HEADS
KC = HID // P
PAIRS = HEADS // 2
GROUP = 4
GTOK = GROUP * SEQ
TURN = 2 * GROUP
BANK = 512
MASKED = -9000000000000000.0
LOWEST = -3.0e38
SCALE = 1.0 / HEAD ** 0.5
EPS = 1e-5

BIAS_AHEAD = 4
X_AHEAD = 2 * GROUP
STORE_LAG = 7
X_RING = 8
V_RING = 4
Y_RING = 4
QK_JOBS = [("q", 0), ("k", 0), ("q", 1), ("k", 1), ("k", 2), ("q", 2)]
QK_STEPS = [[0, 1], [2], [3, 4], [5]]
NJ = len(QK_JOBS)
DMA = 16


def real(n, count=BATCH):
    return not isinstance(n, int) or 0 <= n < count


def past(eng, sem, n, per=1, extra=0):
    value = (n + 1) * per + extra
    if isinstance(value, int) and value <= 0:
        return
    eng.wait_ge(sem, value)


def run_steps(eng, step, last):
    for t in range(-TURN, TURN):
        step(t // TURN, t % TURN)
    with eng.Fori(1, BATCH // TURN - 1) as i:
        for c in range(TURN):
            step(i, c)
    for t in range(BATCH - TURN, last):
        step(t // TURN, t % TURN)


def attention_block(nc, x, adj, wq, bq, wk, bk, wv, bv, wf, bf, out):
    ctx = ExitStack()
    with ctx:
        def sb(name, shape, dt=F32):
            return ctx.enter_context(nc.sbuf_tensor(name, shape, dt))

        def sem(name):
            return ctx.enter_context(nc.semaphore(name))

        x_in = sb("x_in", [P, X_RING, HID])
        x_bias = sb("x_bias", [P, X_RING, HID])
        xT_hi = sb("xT_hi", [P, 2, KC, GTOK], F32R)
        xT_lo = sb("xT_lo", [P, 2, KC, GTOK], F32R)
        w_hi = {m: sb(f"w{m}_hi", [P, KC, HID], F32R) for m in "qkvf"}
        w_lo = {m: sb(f"w{m}_lo", [P, KC, HID], F32R) for m in "qkvf"}
        qT_hi = sb("qT_hi", [P, 2, PAIRS, GTOK], F32R)
        qT_lo = sb("qT_lo", [P, 2, PAIRS, GTOK], F32R)
        kT_hi = sb("kT_hi", [P, 2, PAIRS, GROUP, 2, SEQ], F32R)
        kT_lo = sb("kT_lo", [P, 2, PAIRS, GROUP, 2, SEQ], F32R)
        v_sb = sb("v_sb", [P, V_RING, HID])
        adj_u8 = sb("adj_u8", [P, 2, GROUP, SEQ], U8)
        mask_bias = sb("mask_bias", [P, 2, SEQ])
        s_mask = sb("s_mask", [P, 2, HEADS, SEQ])
        probs = sb("probs", [P, 2, HEADS, SEQ])
        row_max = sb("row_max", [P, 2, HEADS])
        neg_max = sb("neg_max", [P, 2, HEADS])
        row_sum = sb("row_sum", [P, 2, HEADS])
        inv_sum = sb("inv_sum", [P, 2, HEADS])
        pT = sb("pT", [P, HEADS, SEQ])
        cT_hi = sb("cT_hi", [P, KC, SEQ], F32R)
        cT_lo = sb("cT_lo", [P, KC, SEQ], F32R)
        y_sb = sb("y_sb", [P, Y_RING, HID])
        w_raw = {"q": y_sb[:, 0:KC, :], "f": sb("wf_raw", [P, KC, HID])[:, :, :]}
        for m, later in (("k", s_mask), ("v", probs)):
            w_raw[m] = later[:, :, :, :].rearrange("p a h k -> p (a h k)")[:, 0:KC * HID].rearrange(
                "p (c n) -> p c n", n=HID)
        stats = sb("stats", [P, 2, 6])
        mean_var = sb("mean_var", [P, 2, 2])
        var_eps = sb("var_eps", [P, 2, 1])
        rstd = sb("rstd", [P, 2, 1])
        minus_half = sb("minus_half", [P, 1])
        ident = sb("ident", [P, P])
        bq_col = sb("bq_col", [P, KC])
        bk_col = sb("bk_col", [P, KC])
        bv_col = sb("bv_col", [P, KC])
        bv_wide = sb("bv_wide", [P, KC, P])
        bf_row = sb("bf_row", [P, HID])
        bias_row = sb("bias_row", [P, HID])

        def ps(name, banks):
            return ctx.enter_context(nc.psum_tensor(name, [P, banks * BANK], F32))

        scores_ps = ps("scores_ps", 2)
        pT_ps = ps("pT_ps", 2)
        qk_ps = [ps("qk_ps0", 1), ps("qk_ps1", 1)]
        vc_ps = ps("vc_ps", 1)
        ox_ps = ps("ox_ps", 1)

        def apart(eng):
            eng.nop(nofuse=True)

        def heads(h, n=1):
            return slice(h * SEQ, (h + n) * SEQ)

        def x_slot(c):
            n = c + X_AHEAD - 1
            return n // GROUP % 2, slice(n % GROUP * SEQ, (n % GROUP + 1) * SEQ)

        def chunks(ap):
            return ap[:, 0:HID].rearrange("p (c s) -> p c s", c=KC)

        x_loaded = [sem(f"x_loaded{n}") for n in range(X_RING)]
        adj_loaded = [sem(f"adj_loaded{n}") for n in range(2)]
        y_stored = [sem(f"y_stored{n}") for n in range(Y_RING)]
        w_loaded = {m: sem(f"w{m}_loaded") for m in "qkvf"}
        biases_loaded = sem("biases_loaded")
        half_ready = sem("half_ready")
        ident_ready = sem("ident_ready")
        k_zeroed = sem("k_zeroed")
        w_split = {m: sem(f"w{m}_split") for m in "qkvf"}
        w_hi_ready = sem("w_hi_ready")
        wf_hi_ready = sem("wf_hi_ready")
        bv_widened = sem("bv_widened")
        bias_mm = sem("bias_mm")
        bias_row_ready = sem("bias_row_ready")
        scores_done = sem("scores_done")
        pT_done = sem("pT_done")
        v_done = sem("v_done")
        out_done = sem("out_done")
        qk_done = sem("qk_done")
        ctx_done = sem("ctx_done")
        xT_done = sem("xT_done")
        cT_split = sem("cT_split")
        xT_split = sem("xT_split")
        max_found = sem("max_found")
        max_negated = sem("max_negated")
        qk_split = sem("qk_split")
        sum_inverted = sem("sum_inverted")
        y_added = sem("y_added")
        y_stats = sem("y_stats")
        y_aggr = sem("y_aggr")
        var_ready = sem("var_ready")
        cT_hi_ready = sem("cT_hi_ready")
        xT_hi_ready = sem("xT_hi_ready")
        pT_copied = sem("pT_copied")
        exp_done = sem("exp_done")
        v_copied = sem("v_copied")
        qk_hi_ready = sem("qk_hi_ready")
        masked_ready = sem("masked_ready")
        x_biased = sem("x_biased")
        probs_ready = sem("probs_ready")
        rstd_ready = sem("rstd_ready")
        y_ready = sem("y_ready")

        def load_weight(eng, m, w):
            eng.dma_start(w_raw[m][:, :, :], w.rearrange("(c p) n -> p c n", p=P)).then_inc(w_loaded[m], DMA)

        block = ctx.enter_context(nc.Block())

        @block.sync
        def _(sp):
            def step(i, c):
                t = TURN * i + c
                g = 2 * i + c // GROUP
                if c % GROUP == 0 and real(g, BATCH // GROUP):
                    past(sp, masked_ready, (g - 1) * GROUP - 1)
                    sp.dma_start(adj_u8[:, c // GROUP, :, :],
                                 adj[bass.ds(g * GROUP, GROUP), :, :].rearrange("b q k -> q b k")
                                 ).then_inc(adj_loaded[c // GROUP], DMA)
                n = t + X_AHEAD
                if isinstance(n, int) and n == GROUP:
                    load_weight(sp, "k", wk)
                    sp.wait_ge(w_loaded["k"], DMA)
                if real(n):
                    past(sp, x_biased, n - X_RING)
                    past(sp, xT_done, n - X_RING)
                    sp.dma_start(x_in[:, c, :], x[bass.ds(n, 1), :, :].rearrange("b p d -> p (b d)")
                                 ).then_inc(x_loaded[c], DMA)
                n = t - STORE_LAG
                if real(n):
                    past(sp, y_ready, n)
                    sp.dma_start(out[bass.ds(n, 1), :, :].rearrange("b p d -> p (b d)"),
                                 y_sb[:, (c - STORE_LAG) % Y_RING, :]
                                 ).then_inc(y_stored[(c - STORE_LAG) % Y_RING], DMA)

            run_steps(sp, step, BATCH + STORE_LAG)
            for slot in range(Y_RING):
                sp.wait_ge(y_stored[slot], DMA * (BATCH // Y_RING))

        @block.tensor
        def _(pe):
            def split_product(dst, pairs, done, n_chunks=KC):
                for k in range(n_chunks):
                    s_hi, s_lo, m_hi, m_lo = pairs(k)
                    nc.tensor.matmul(dst, s_hi, m_hi, start=k == 0, stop=False)
                    nc.tensor.matmul(dst, s_hi, m_lo, start=False, stop=False)
                    last = nc.tensor.matmul(dst, s_lo, m_hi, start=False, stop=k == n_chunks - 1)
                last.then_inc(done, 1)

            def scores(i, c, t):
                g = 2 * i + c // GROUP
                par, b = c // GROUP, c % GROUP
                past(pe, qk_split, g, per=NJ)
                past(pe, max_found, t - 1)
                for m in range(PAIRS):
                    dst = scores_ps[:, heads(2 * m, 2)]
                    q_hi, q_lo = (w[:, par, m, b * SEQ:(b + 1) * SEQ] for w in (qT_hi, qT_lo))
                    k_hi, k_lo = (w[:, par, m, b, :, :].rearrange("p a k -> p (a k)") for w in (kT_hi, kT_lo))
                    nc.tensor.matmul(dst, q_hi, k_hi, start=True, stop=False)
                    nc.tensor.matmul(dst, q_hi, k_lo, start=False, stop=False)
                    last = nc.tensor.matmul(dst, q_lo, k_hi, start=False, stop=True)
                last.then_inc(scores_done, 1)

            def transpose_probs(c, n):
                slot = (c - 1) % 2
                past(pe, probs_ready, n)
                past(pe, pT_copied, n - 1)
                for h in range(HEADS):
                    last = nc.tensor.transpose(pT_ps[:, heads(h)], probs[:, slot, h, :], ident[:, :])
                last.then_inc(pT_done, 1)

            def v_product(c, t):
                par, b = c // GROUP, c % GROUP
                past(pe, xT_split, t)
                if isinstance(t, int) and t < 2:
                    past(pe, v_copied, t - 1)
                else:
                    past(pe, cT_split, t - 2)
                split_product(vc_ps[:, 0:HID], lambda k: (
                    xT_hi[:, par, k, b * SEQ:(b + 1) * SEQ], xT_lo[:, par, k, b * SEQ:(b + 1) * SEQ],
                    w_hi["v"][:, k, :], w_lo["v"][:, k, :]), v_done)

            def out_product(t, n):
                past(pe, cT_split, n)
                if isinstance(t, int) and t + X_AHEAD - 1 >= BATCH:
                    past(pe, y_added, n - 1)
                else:
                    past(pe, xT_split, t + X_AHEAD - 1)
                split_product(ox_ps[:, 0:HID], lambda k: (
                    cT_hi[:, k, :], cT_lo[:, k, :], w_hi["f"][:, k, :], w_lo["f"][:, k, :]), out_done)

            def qk_product(i, c, g, j):
                mat, m = QK_JOBS[j]
                par = (c // GROUP + 1) % 2
                past(pe, xT_split, g * GROUP + GROUP - 1)
                past(pe, qk_split, g * NJ + j - 2)
                split_product(qk_ps[j % 2][:, :], lambda k: (
                    w_hi[mat][:, k, m * P:(m + 1) * P], w_lo[mat][:, k, m * P:(m + 1) * P],
                    xT_hi[:, par, k, :], xT_lo[:, par, k, :]), qk_done)

            def ctx_product(c, t, n):
                slot = (c - 2) % V_RING
                past(pe, pT_copied, n)
                if isinstance(t, int) and t > BATCH:
                    past(pe, cT_split, n - 1)
                past(pe, v_copied, min(t, BATCH) - 1 if isinstance(t, int) else t - 1)
                for h in range(HEADS):
                    half = h % 2 * HEAD
                    last = nc.tensor.matmul(vc_ps[half:half + HEAD, h // 2 * SEQ:(h // 2 + 1) * SEQ],
                                            v_sb[:, slot, h * HEAD:(h + 1) * HEAD], pT[:, h, :],
                                            start=True, stop=True)
                last.then_inc(ctx_done, 1)

            def transpose_x(i, c, t, n):
                past(pe, x_loaded[c], i + 1, per=DMA)
                if isinstance(t, int) and t < 2:
                    past(pe, xT_split, n - 1)
                else:
                    past(pe, y_added, t - 2)
                for k in range(KC):
                    last = nc.tensor.transpose(ox_ps[:, k * SEQ:(k + 1) * SEQ],
                                               x_in[:, c, k * P:(k + 1) * P], ident[:, :])
                last.then_inc(xT_done, 1)

            def bias_product():
                pe.wait_ge(w_loaded["f"], DMA)
                pe.wait_ge(bv_widened, 1)
                for k in range(KC):
                    last = nc.tensor.matmul(pT_ps[:, 0:HID], bv_wide[:, k, :], w_raw["f"][:, k, :],
                                            start=k == 0, stop=k == KC - 1)
                last.then_inc(bias_mm, 1)

            def step(i, c):
                t = TURN * i + c
                g = 2 * i + c // GROUP + 1
                drained = isinstance(t, int) and t + 1 >= BATCH
                if drained:
                    ctx_product(c, t, t - 2)
                if real(t):
                    scores(i, c, t)
                if real(t - 2) and not drained:
                    ctx_product(c, t, t - 2)
                if real(t - 1):
                    transpose_probs(c, t - 1)
                if isinstance(t, int) and t == -GROUP:
                    pe.wait_ge(w_split["q"], 1)
                    pe.wait_ge(w_split["k"], 1)
                if real(g, BATCH // GROUP):
                    for j in QK_STEPS[c % GROUP]:
                        qk_product(i, c, g, j)
                if isinstance(t, int) and t == -1:
                    bias_product()
                if isinstance(t, int) and t == 2:
                    pe.wait_ge(w_split["f"], 1)
                if real(t - 2):
                    out_product(t, t - 2)
                if isinstance(t, int) and t == 0:
                    pe.wait_ge(w_split["v"], 1)
                if real(t):
                    v_product(c, t)
                if real(t + X_AHEAD):
                    transpose_x(i, c, t, t + X_AHEAD)

            pe.wait_ge(ident_ready, 2)
            run_steps(pe, step, BATCH + 2)

        @block.vector
        def _(dve):
            def split_weight(m):
                dve.wait_ge(w_hi_ready, "qkv".index(m) + 1)
                nc.vector.tensor_tensor(w_lo[m][:, :, :], w_raw[m][:, :, :], w_hi[m][:, :, :].bitcast(F32),
                                        ALU.subtract).then_inc(w_split[m], 1)

            def split_ctx(n):
                past(dve, cT_hi_ready, n)
                nc.vector.tensor_tensor(cT_lo[:, :, :], chunks(vc_ps), cT_hi[:, :, :].bitcast(F32),
                                        ALU.subtract).then_inc(cT_split, 1)

            def split_x(i, c, n):
                par, b = x_slot(c)
                past(dve, xT_hi_ready, n)
                nc.vector.tensor_tensor(xT_lo[:, par, :, b], chunks(ox_ps),
                                        xT_hi[:, par, :, b].bitcast(F32), ALU.subtract).then_inc(xT_split, 1)

            def mask_and_max(c, t):
                slot = c % 2
                past(dve, scores_done, t)
                past(dve, masked_ready, t)
                past(dve, exp_done, t - 2)
                apart(dve)
                for h in range(HEADS):
                    last = nc.vector.tensor_tensor_reduce(
                        out=s_mask[:, slot, h, :], in0=scores_ps[:, heads(h)], in1=mask_bias[:, slot, :],
                        scale=SCALE, scalar=LOWEST, op0=ALU.add, op1=ALU.max,
                        accum_out=row_max[:, slot, h:h + 1])
                last.then_inc(max_found, 1)
                past(dve, max_found, t)
                nc.vector.tensor_scalar(neg_max[:, slot, :], row_max[:, slot, :], -1.0, None, ALU.mult
                                        ).then_inc(max_negated, 1)

            def split_qk(c, g, j):
                mat, m = QK_JOBS[j]
                par = (c // GROUP + 1) % 2
                past(dve, qk_hi_ready, g * NJ + j)
                src = qk_ps[j % 2]
                if mat == "q":
                    nc.vector.scalar_tensor_tensor(
                        out=qT_lo[:, par, m, :], in0=src[:, :], scalar=bq_col[:, m:m + 1],
                        in1=qT_hi[:, par, m, :].bitcast(F32), op0=ALU.add, op1=ALU.subtract).then_inc(qk_split, 1)
                    return
                for half in range(2):
                    rows = slice(half * HEAD, (half + 1) * HEAD)
                    last = nc.vector.scalar_tensor_tensor(
                        out=kT_lo[rows, par, m, :, half, :], in0=src[rows, :].rearrange("p (b k) -> p b k", k=SEQ),
                        scalar=bk_col[rows, m:m + 1], in1=kT_hi[rows, par, m, :, half, :].bitcast(F32),
                        op0=ALU.add, op1=ALU.subtract)
                last.then_inc(qk_split, 1)

            def invert_sums(c, t):
                slot = c % 2
                past(dve, exp_done, t)
                past(dve, probs_ready, t - 2)
                nc.vector.reciprocal(inv_sum[:, slot, :], row_sum[:, slot, :]).then_inc(sum_inverted, 1)

            def residual_and_stats(i, c, n):
                slot, y = c % 2, (c - 2) % Y_RING
                past(dve, out_done, n)
                past(dve, x_biased, n)
                if isinstance(n, int):
                    if n >= Y_RING:
                        dve.wait_ge(y_stored[y], DMA * (n // Y_RING))
                else:
                    dve.wait_ge(y_stored[y], (2 * i + (c - 2) // Y_RING) * DMA)
                nc.vector.tensor_tensor(y_sb[:, y, :], ox_ps[:, 0:HID], x_bias[:, (c - 2) % X_RING, :], ALU.add
                                        ).then_inc(y_added, 1)
                past(dve, y_added, n)
                nc.vector.bn_stats(stats[:, slot, :], y_sb[:, y, :]).then_inc(y_stats, 1)
                past(dve, y_stats, n)
                past(dve, y_ready, n - 2)
                apart(dve)
                nc.vector.bn_aggr(mean_var[:, slot, :], stats[:, slot, :]).then_inc(y_aggr, 1)
                past(dve, y_aggr, n)
                nc.vector.tensor_scalar(var_eps[:, slot, :], mean_var[:, slot, 1:2], EPS, None, ALU.add
                                        ).then_inc(var_ready, 1)

            def step(i, c):
                t = TURN * i + c
                g = 2 * i + c // GROUP + 1
                if isinstance(t, int) and t == -GROUP - 1:
                    dve.wait_ge(biases_loaded, 4 * DMA)
                    nc.vector.tensor_copy(bv_wide[:, :, :], bv_col[:, :].unsqueeze(2).broadcast_to([P, KC, P])
                                          ).then_inc(bv_widened, 1)
                urgent = c % GROUP == 0
                if real(t + X_AHEAD - 1) and urgent:
                    split_x(i, c, t + X_AHEAD - 1)
                if isinstance(t, int) and t == -GROUP:
                    split_weight("q")
                    split_weight("k")
                if isinstance(t, int) and t == 2 - GROUP:
                    split_weight("v")
                if isinstance(t, int) and t == -1:
                    dve.wait_ge(bias_mm, 1)
                    nc.vector.tensor_tensor(bias_row[:, :], pT_ps[:, 0:HID], bf_row[:, :], ALU.add
                                            ).then_inc(bias_row_ready, 1)
                if real(t):
                    mask_and_max(c, t)
                if real(t + X_AHEAD - 1) and not urgent:
                    split_x(i, c, t + X_AHEAD - 1)
                if real(t - 2):
                    split_ctx(t - 2)
                if real(t):
                    invert_sums(c, t)
                jobs = QK_STEPS[c % GROUP] if real(g, BATCH // GROUP) else []
                before = jobs if c % GROUP == GROUP - 1 else jobs[:-1]
                for j in before:
                    split_qk(c, g, j)
                if real(t - 2):
                    residual_and_stats(i, c, t - 2)
                for j in jobs[len(before):]:
                    split_qk(c, g, j)

            run_steps(dve, step, BATCH + 2)

        @block.scalar
        def _(act):
            load_weight(act, "q", wq)
            for dst, b in ((bq_col, bq), (bk_col, bk), (bv_col, bv)):
                act.dma_start(dst[:, :], b.rearrange("(c p) -> p c", p=P), allow_slow_non_contiguous=True).then_inc(biases_loaded, DMA)
            act.dma_start(bf_row[:, :], bf.rearrange("(a n) -> a n", a=1).broadcast_to([P, HID])
                          ).then_inc(biases_loaded, DMA)

            def round_weight(m):
                act.wait_ge(w_loaded[m], DMA)
                nc.scalar.copy(w_hi[m][:, :, :], w_raw[m][:, :, :]).then_inc(w_hi_ready, 1)

            def round_x(i, c, n):
                g = 2 * i + 1 + (c + 3) // GROUP
                par, b = x_slot(c)
                past(act, xT_done, n)
                past(act, qk_done, g - 2, per=NJ)
                past(act, v_done, n - TURN)
                nc.scalar.copy(xT_hi[:, par, :, b], chunks(ox_ps)).then_inc(xT_hi_ready, 1)

            def round_ctx(n):
                past(act, ctx_done, n)
                past(act, out_done, n - 1)
                nc.scalar.copy(cT_hi[:, :, :], chunks(vc_ps)).then_inc(cT_hi_ready, 1)

            def copy_pT(n):
                past(act, pT_done, n)
                past(act, ctx_done, n - 1)
                nc.scalar.copy(pT[:, :, :].rearrange("p h q -> p (h q)"), pT_ps[:, heads(0, HEADS)]
                               ).then_inc(pT_copied, 1)

            def exps(c, t):
                slot = c % 2
                past(act, max_negated, t)
                past(act, pT_done, t - 2)
                for h in range(HEADS):
                    last = nc.scalar.activation(probs[:, slot, h, :], s_mask[:, slot, h, :], ACT.Exp,
                                                bias=neg_max[:, slot, h:h + 1], scale=1.0,
                                                accum_out=row_sum[:, slot, h:h + 1])
                last.then_inc(exp_done, 1)

            def copy_v(c, n):
                slot = c % V_RING
                past(act, v_done, n)
                past(act, ctx_done, n - V_RING)
                nc.scalar.copy(v_sb[:, slot, :], vc_ps[:, 0:HID]).then_inc(v_copied, 1)

            def round_qk(c, g, j):
                mat, m = QK_JOBS[j]
                par = (c // GROUP + 1) % 2
                past(act, qk_done, g * NJ + j)
                past(act, scores_done, (g - 1) * GROUP - 1)
                src = qk_ps[j % 2]
                if mat == "q":
                    nc.scalar.activation(qT_hi[:, par, m, :], src[:, :], ACT.Identity,
                                         bias=bq_col[:, m:m + 1], scale=1.0).then_inc(qk_hi_ready, 1)
                    return
                for half in range(2):
                    rows = slice(half * HEAD, (half + 1) * HEAD)
                    last = nc.scalar.activation(kT_hi[rows, par, m, :, half, :],
                                                src[rows, :].rearrange("p (b k) -> p b k", k=SEQ), ACT.Identity,
                                                bias=bk_col[rows, m:m + 1], scale=1.0)
                last.then_inc(qk_hi_ready, 1)

            def step(i, c):
                t = TURN * i + c
                g = 2 * i + c // GROUP + 1
                if real(t + X_AHEAD - 1):
                    round_x(i, c, t + X_AHEAD - 1)
                if isinstance(t, int) and t == -GROUP:
                    round_weight("q")
                    round_weight("k")
                    load_weight(act, "f", wf)
                    load_weight(act, "v", wv)
                if isinstance(t, int) and t == 2 - GROUP:
                    round_weight("v")
                if real(t - 2):
                    round_ctx(t - 2)
                if real(t):
                    exps(c, t)
                if isinstance(t, int) and t == -GROUP:
                    act.wait_ge(biases_loaded, 4 * DMA)
                    act.wait_ge(k_zeroed, 2)
                jobs = QK_STEPS[c % GROUP] if real(g, BATCH // GROUP) else []
                for j in jobs[:1]:
                    round_qk(c, g, j)
                if real(t - 1):
                    copy_pT(t - 1)
                for j in jobs[1:]:
                    round_qk(c, g, j)
                if real(t):
                    copy_v(c, t)

            run_steps(act, step, BATCH + 2)

        @block.gpsimd
        def _(pool):
            nc.gpsimd.memset(minus_half[:, :], -0.5).then_inc(half_ready, 1)
            nc.gpsimd.memset(ident[:, :], 0.0).then_inc(ident_ready, 1)
            pool.wait_ge(ident_ready, 1)
            nc.gpsimd.affine_select(out=ident[:, :], in_=ident[:, :], compare_op=ALU.not_equal, fill=1.0,
                                    base=0, pattern=[[-1, P]], channel_multiplier=1).then_inc(ident_ready, 1)
            for part in (kT_hi, kT_lo):
                nc.gpsimd.memset(part[:, :, :, :, :, :].bitcast(F32), 0.0).then_inc(k_zeroed, 1)
            pool.wait_ge(w_loaded["f"], DMA)
            nc.gpsimd.tensor_copy(w_hi["f"][:, :, :], w_raw["f"][:, :, :]).then_inc(wf_hi_ready, 1)
            pool.wait_ge(wf_hi_ready, 1)
            nc.gpsimd.tensor_tensor(w_lo["f"][:, :, :], w_raw["f"][:, :, :], w_hi["f"][:, :, :].bitcast(F32),
                                    ALU.subtract).then_inc(w_split["f"], 1)

            pool.wait_ge(half_ready, 1)

            def make_mask_bias(i, c, n):
                b = (c + 1) % GROUP
                par = (c + 1) // GROUP % 2
                past(pool, adj_loaded[par], i + (c + 1) // TURN, per=DMA)
                past(pool, max_found, n - 2)
                apart(pool)
                nc.gpsimd.tensor_scalar(mask_bias[:, (c + 1) % 2, :], adj_u8[:, par, b, :], -MASKED / SCALE, MASKED / SCALE,
                                        ALU.mult, ALU.add).then_inc(masked_ready, 1)

            def add_bias(i, c, n):
                slot = (c + BIAS_AHEAD) % X_RING
                past(pool, x_loaded[slot], i + (c + BIAS_AHEAD) // TURN, per=DMA)
                past(pool, y_added, n - X_RING)
                nc.gpsimd.tensor_tensor(x_bias[:, slot, :], x_in[:, slot, :], bias_row[:, :], ALU.add
                                        ).then_inc(x_biased, 1)

            def normalise_y(c, n):
                slot, y = c % 2, (c - 2) % Y_RING
                past(pool, var_ready, n)
                nc.gpsimd.tensor_tensor(rstd[:, slot, :], var_eps[:, slot, :], minus_half[:, :], ALU.pow
                                        ).then_inc(rstd_ready, 1)
                past(pool, rstd_ready, n)
                apart(pool)
                nc.gpsimd.tensor_scalar(y_sb[:, y, :], y_sb[:, y, :], mean_var[:, slot, 0:1], rstd[:, slot, 0:1],
                                        ALU.subtract, ALU.mult).then_inc(y_ready, 1)

            def normalise_probs(c, t):
                slot = c % 2
                past(pool, sum_inverted, t)
                nc.gpsimd.tensor_tensor(probs[:, slot, :, :], probs[:, slot, :, :],
                                        inv_sum[:, slot, :].unsqueeze(2).broadcast_to([P, HEADS, SEQ]), ALU.mult
                                        ).then_inc(probs_ready, 1)

            def step(i, c):
                t = TURN * i + c
                if real(t + 1):
                    make_mask_bias(i, c, t + 1)
                if isinstance(t, int) and t == -BIAS_AHEAD:
                    pool.wait_ge(bias_row_ready, 1)
                if real(t + BIAS_AHEAD):
                    add_bias(i, c, t + BIAS_AHEAD)
                if real(t):
                    normalise_probs(c, t)
                if real(t - 2):
                    normalise_y(c, t - 2)

            run_steps(pool, step, BATCH + 2)


_INS = ["x", "adj", "L0_gnn_Wq", "L0_gnn_bq", "L0_gnn_Wk", "L0_gnn_bk", "L0_gnn_Wv", "L0_gnn_bv",
        "L0_gnn_Wf", "L0_gnn_bf"]


def kernel(**inputs):
    import numpy as _np
    import concourse.bacc as _bacc
    from concourse import mybir as _mybir
    from concourse.bass_utils import run_bass_kernel_spmd as _run

    nc = _bacc.Bacc("TRN2", target_bir_lowering=False, num_devices=1)
    arrays, args = {}, []
    for name in _INS:
        a = _np.ascontiguousarray(inputs[name])
        arrays[f"in_{name}"] = a
        args.append(nc.dram_tensor(f"in_{name}", a.shape, _mybir.dt.from_np(a.dtype), kind="ExternalInput").ap())
    out = nc.dram_tensor("out_0", (BATCH, SEQ, HID), F32, kind="ExternalOutput").ap()
    attention_block(nc, *args, out)
    r = _run(nc, [arrays], core_ids=[0])
    return r.results[0]["out_0"]
```

```python
from contextlib import ExitStack

import concourse.bass as bass
from concourse import mybir

ALU = mybir.AluOpType
ACT = mybir.ActivationFunctionType
AX = mybir.AxisListType
F32 = mybir.dt.float32
F32R = mybir.dt.float32r
U8 = mybir.dt.uint8

P = 128
BATCH = 128
SEQ = 128
HID = 384
HEADS = 6
HEAD = HID // HEADS
KC = HID // P
PAIRS = HEADS // 2
GROUP = 4
GTOK = GROUP * SEQ
TURN = 2 * GROUP
BANK = 512
MASKED = -9000000000000000.0
LOWEST = -3.0e38
SCALE = 1.0 / HEAD ** 0.5
EPS = 1e-5

BIAS_AHEAD = 4
X_AHEAD = 2 * GROUP
STORE_LAG = 7
X_RING = 8
V_RING = 4
Y_RING = 4
QK_JOBS = [("q", 0), ("k", 0), ("q", 1), ("k", 1), ("k", 2), ("q", 2)]
QK_STEPS = [[0, 1], [2], [3, 4], [5]]
NJ = len(QK_JOBS)
WARM_UPS = {-1: 8, 0: 7, 3: 12}
DMA = 16


def real(n, count=BATCH):
    return not isinstance(n, int) or 0 <= n < count


def in_tail(t):
    return isinstance(t, int) and t >= BATCH - GROUP


def past(eng, sem, n, per=1, extra=0):
    value = (n + 1) * per + extra
    if isinstance(value, int) and value <= 0:
        return
    eng.wait_ge(sem, value)


def run_steps(eng, step, last):
    for t in range(-TURN, TURN):
        step(t // TURN, t % TURN)
    with eng.Fori(1, BATCH // TURN - 1) as i:
        for c in range(TURN):
            step(i, c)
    for t in range(BATCH - TURN, last):
        step(t // TURN, t % TURN)


def attention_block(nc, x, adj, wq, bq, wk, bk, wv, bv, wf, bf, out):
    ctx = ExitStack()
    with ctx:
        def sb(name, shape, dt=F32):
            return ctx.enter_context(nc.sbuf_tensor(name, shape, dt))

        def sem(name):
            return ctx.enter_context(nc.semaphore(name))

        x_in = sb("x_in", [P, X_RING, HID])
        x_bias = sb("x_bias", [P, X_RING, HID])
        xT_hi = sb("xT_hi", [P, 2, KC, GTOK], F32R)
        xT_lo = sb("xT_lo", [P, 2, KC, GTOK], F32R)
        w_hi = {m: sb(f"w{m}_hi", [P, KC, HID], F32R) for m in "qkvf"}
        w_lo = {m: sb(f"w{m}_lo", [P, KC, HID], F32R) for m in "qkvf"}
        qT_hi = sb("qT_hi", [P, 2, PAIRS, GTOK], F32R)
        qT_lo = sb("qT_lo", [P, 2, PAIRS, GTOK], F32R)
        kT_hi = sb("kT_hi", [P, 2, PAIRS, GROUP, 2, SEQ], F32R)
        kT_lo = sb("kT_lo", [P, 2, PAIRS, GROUP, 2, SEQ], F32R)
        v_sb = sb("v_sb", [P, V_RING, HID])
        adj_u8 = sb("adj_u8", [P, 2, GROUP, SEQ], U8)
        mask_bias = sb("mask_bias", [P, 2, SEQ])
        s_mask = sb("s_mask", [P, 2, HEADS, SEQ])
        probs = sb("probs", [P, 2, HEADS, SEQ])
        row_max = sb("row_max", [P, 2, HEADS])
        neg_max = sb("neg_max", [P, 2, HEADS])
        row_sum = sb("row_sum", [P, 2, HEADS])
        inv_sum = sb("inv_sum", [P, 2, HEADS])
        pT = sb("pT", [P, HEADS, SEQ])
        cT_hi = sb("cT_hi", [P, KC, SEQ], F32R)
        cT_lo = sb("cT_lo", [P, KC, SEQ], F32R)
        y_sb = sb("y_sb", [P, Y_RING, HID])
        w_raw = {"q": y_sb[:, 0:KC, :], "f": sb("wf_raw", [P, KC, HID])[:, :, :]}
        for m, later in (("k", s_mask), ("v", probs)):
            w_raw[m] = later[:, :, :, :].rearrange("p a h k -> p (a h k)")[:, 0:KC * HID].rearrange(
                "p (c n) -> p c n", n=HID)
        stats = sb("stats", [P, 2, 6])
        mean_var = sb("mean_var", [P, 2, 2])
        var_eps = sb("var_eps", [P, 2, 1])
        rstd = sb("rstd", [P, 2, 1])
        minus_half = sb("minus_half", [P, 1])
        ident = sb("ident", [P, P])
        bq_col = sb("bq_col", [P, KC])
        bk_col = sb("bk_col", [P, KC])
        bv_col = sb("bv_col", [P, KC])
        bv_wide = sb("bv_wide", [P, KC, P])
        bf_row = sb("bf_row", [P, HID])
        bias_row = sb("bias_row", [P, HID])

        def ps(name, banks):
            return ctx.enter_context(nc.psum_tensor(name, [P, banks * BANK], F32))

        scores_ps = ps("scores_ps", 2)
        pT_ps = ps("pT_ps", 2)
        qk_ps = [ps("qk_ps0", 1), ps("qk_ps1", 1)]
        vc_ps = ps("vc_ps", 1)
        ox_ps = ps("ox_ps", 1)

        def apart(eng):
            eng.nop(nofuse=True)

        def heads(h, n=1):
            return slice(h * SEQ, (h + n) * SEQ)

        def x_slot(c):
            n = c + X_AHEAD - 1
            return n // GROUP % 2, slice(n % GROUP * SEQ, (n % GROUP + 1) * SEQ)

        def xT_bank(n):
            if isinstance(n, int) and n < TURN:
                return [ox_ps[:, :], vc_ps[:, :], pT_ps[:, 0:BANK], pT_ps[:, BANK:2 * BANK]][n % 4]
            return ox_ps[:, :]

        def v_bank(n):
            return qk_ps[n % 2][:, :] if in_tail(n) else vc_ps[:, :]

        def chunks(ap):
            return ap[:, 0:HID].rearrange("p (c s) -> p c s", c=KC)

        x_loaded = [sem(f"x_loaded{n}") for n in range(X_RING)]
        adj_loaded = [sem(f"adj_loaded{n}") for n in range(2)]
        y_stored = [sem(f"y_stored{n}") for n in range(Y_RING)]
        w_loaded = {m: sem(f"w{m}_loaded") for m in "qkvf"}
        biases_loaded = sem("biases_loaded")
        half_ready = sem("half_ready")
        ident_ready = sem("ident_ready")
        k_zeroed = sem("k_zeroed")
        w_split = {m: sem(f"w{m}_split") for m in "qkvf"}
        w_hi_ready = {m: sem(f"w{m}_hi_ready") for m in "qkvf"}
        bv_widened = sem("bv_widened")
        bias_mm = sem("bias_mm")
        bias_row_ready = sem("bias_row_ready")
        scores_done = sem("scores_done")
        pT_done = sem("pT_done")
        v_done = sem("v_done")
        out_done = sem("out_done")
        qk_done = sem("qk_done")
        ctx_done = sem("ctx_done")
        xT_done = sem("xT_done")
        cT_split = sem("cT_split")
        xT_split = sem("xT_split")
        max_found = sem("max_found")
        max_negated = sem("max_negated")
        qk_split = sem("qk_split")
        sum_inverted = sem("sum_inverted")
        y_added = sem("y_added")
        y_stats = sem("y_stats")
        y_aggr = sem("y_aggr")
        var_ready = sem("var_ready")
        cT_hi_ready = sem("cT_hi_ready")
        xT_hi_ready = sem("xT_hi_ready")
        pT_copied = sem("pT_copied")
        exp_done = sem("exp_done")
        v_copied = sem("v_copied")
        qk_hi_ready = sem("qk_hi_ready")
        masked_ready = sem("masked_ready")
        x_biased = sem("x_biased")
        probs_ready = sem("probs_ready")
        rstd_ready = sem("rstd_ready")
        y_ready = sem("y_ready")
        last_y_ready = sem("last_y_ready")

        def load_weight(eng, m, w):
            eng.dma_start(w_raw[m][:, :, :], w.rearrange("(c p) n -> p c n", p=P)).then_inc(w_loaded[m], DMA)

        def load_biases(eng):
            for dst, b in ((bq_col, bq), (bk_col, bk), (bv_col, bv)):
                eng.dma_start(dst[:, :], b.rearrange("(c p) -> p c", p=P), allow_slow_non_contiguous=True
                              ).then_inc(biases_loaded, DMA)
            eng.dma_start(bf_row[:, :], bf.rearrange("(a n) -> a n", a=1).broadcast_to([P, HID])
                          ).then_inc(biases_loaded, DMA)

        block = ctx.enter_context(nc.Block())

        @block.sync
        def _(sp):
            def step(i, c):
                t = TURN * i + c
                g = 2 * i + c // GROUP
                if c % GROUP == 0 and real(g, BATCH // GROUP):
                    past(sp, masked_ready, (g - 1) * GROUP - 1)
                    sp.dma_start(adj_u8[:, c // GROUP, :, :],
                                 adj[bass.ds(g * GROUP, GROUP), :, :].rearrange("b q k -> q b k")
                                 ).then_inc(adj_loaded[c // GROUP], DMA)
                n = t + X_AHEAD
                if isinstance(n, int) and n == GROUP:
                    load_weight(sp, "k", wk)
                    load_biases(sp)
                    sp.wait_ge(w_loaded["k"], DMA)
                if isinstance(n, int) and n == TURN:
                    load_weight(sp, "v", wv)
                    load_weight(sp, "f", wf)
                if real(n):
                    past(sp, x_biased, n - X_RING)
                    past(sp, xT_done, n - X_RING)
                    sp.dma_start(x_in[:, c, :], x[bass.ds(n, 1), :, :].rearrange("b p d -> p (b d)")
                                 ).then_inc(x_loaded[c], DMA)
                n = t - STORE_LAG
                if real(n):
                    if isinstance(n, int) and n == BATCH - 1:
                        sp.wait_ge(last_y_ready, 1)
                    else:
                        past(sp, y_ready, n)
                    sp.dma_start(out[bass.ds(n, 1), :, :].rearrange("b p d -> p (b d)"),
                                 y_sb[:, (c - STORE_LAG) % Y_RING, :]
                                 ).then_inc(y_stored[(c - STORE_LAG) % Y_RING], DMA)

            run_steps(sp, step, BATCH + STORE_LAG)
            for slot in range(Y_RING):
                sp.wait_ge(y_stored[slot], DMA * (BATCH // Y_RING))

        @block.tensor
        def _(pe):
            def split_product(dst, pairs, done, n_chunks=KC):
                for k in range(n_chunks):
                    s_hi, s_lo, m_hi, m_lo = pairs(k)
                    nc.tensor.matmul(dst, s_hi, m_hi, start=k == 0, stop=False)
                    nc.tensor.matmul(dst, s_hi, m_lo, start=False, stop=False)
                    last = nc.tensor.matmul(dst, s_lo, m_hi, start=False, stop=k == n_chunks - 1)
                last.then_inc(done, 1)

            def scores(i, c, t):
                g = 2 * i + c // GROUP
                par, b = c // GROUP, c % GROUP
                past(pe, qk_split, g, per=NJ)
                if isinstance(t, int) and t == 0:
                    pe.wait_ge(bias_row_ready, 1)
                past(pe, max_found, t - 1)
                for m in range(PAIRS):
                    dst = scores_ps[:, heads(2 * m, 2)]
                    q_hi, q_lo = (w[:, par, m, b * SEQ:(b + 1) * SEQ] for w in (qT_hi, qT_lo))
                    k_hi, k_lo = (w[:, par, m, b, :, :].rearrange("p a k -> p (a k)") for w in (kT_hi, kT_lo))
                    nc.tensor.matmul(dst, q_hi, k_hi, start=True, stop=False)
                    nc.tensor.matmul(dst, q_hi, k_lo, start=False, stop=False)
                    last = nc.tensor.matmul(dst, q_lo, k_hi, start=False, stop=True)
                last.then_inc(scores_done, 1)

            def transpose_probs(c, n):
                slot = (c - 1) % 2
                past(pe, probs_ready, n)
                if isinstance(n, int) and n == 0:
                    past(pe, xT_split, TURN - 1)
                past(pe, pT_copied, n - 1)
                for h in range(HEADS):
                    last = nc.tensor.transpose(pT_ps[:, heads(h)], probs[:, slot, h, :], ident[:, :])
                last.then_inc(pT_done, 1)

            def v_product(c, t):
                par, b = c // GROUP, c % GROUP
                if isinstance(t, int) and t == 0:
                    past(pe, xT_split, 5)
                else:
                    past(pe, xT_split, t)
                    if in_tail(t):
                        past(pe, v_copied, t - 2)
                    elif isinstance(t, int) and t == 1:
                        past(pe, v_copied, t - 1)
                    else:
                        past(pe, cT_split, t - 2)
                split_product(v_bank(t)[:, 0:HID], lambda k: (
                    xT_hi[:, par, k, b * SEQ:(b + 1) * SEQ], xT_lo[:, par, k, b * SEQ:(b + 1) * SEQ],
                    w_hi["v"][:, k, :], w_lo["v"][:, k, :]), v_done)

            def out_product(t, n):
                past(pe, cT_split, n)
                if isinstance(t, int) and t + X_AHEAD - 1 >= BATCH:
                    past(pe, y_added, n - 1)
                else:
                    past(pe, xT_split, t + X_AHEAD - 1)
                split_product(ox_ps[:, 0:HID], lambda k: (
                    cT_hi[:, k, :], cT_lo[:, k, :], w_hi["f"][:, k, :], w_lo["f"][:, k, :]), out_done)

            def qk_product(i, c, g, j):
                mat, m = QK_JOBS[j]
                par = (c // GROUP + 1) % 2
                if isinstance(g, int) and g == 0:
                    past(pe, w_split[mat], m)
                past(pe, xT_split, g * GROUP + GROUP - 1)
                past(pe, qk_split, g * NJ + j - 2)
                split_product(qk_ps[j % 2][:, :], lambda k: (
                    w_hi[mat][:, k, m * P:(m + 1) * P], w_lo[mat][:, k, m * P:(m + 1) * P],
                    xT_hi[:, par, k, :], xT_lo[:, par, k, :]), qk_done)

            def ctx_product(c, t, n):
                slot = (c - 2) % V_RING
                past(pe, pT_copied, n)
                if in_tail(t - 1):
                    past(pe, v_copied, n)
                    past(pe, cT_split, n - 1)
                else:
                    past(pe, v_copied, t - 1)
                for h in range(HEADS):
                    half = h % 2 * HEAD
                    last = nc.tensor.matmul(vc_ps[half:half + HEAD, h // 2 * SEQ:(h // 2 + 1) * SEQ],
                                            v_sb[:, slot, h * HEAD:(h + 1) * HEAD], pT[:, h, :],
                                            start=True, stop=True)
                last.then_inc(ctx_done, 1)

            def transpose_x(i, c, t, n):
                past(pe, x_loaded[c], i + 1, per=DMA)
                if isinstance(t, int) and t < 2:
                    past(pe, xT_split, n - 4 if n <= TURN else n - 1)
                else:
                    past(pe, y_added, t - 2)
                for k in range(KC):
                    last = nc.tensor.transpose(xT_bank(n)[:, k * SEQ:(k + 1) * SEQ],
                                               x_in[:, c, k * P:(k + 1) * P], ident[:, :])
                last.then_inc(xT_done, 1)

            def warm_up(n):
                for _ in range(n):
                    nc.tensor.transpose(qk_ps[1][:, 0:P], ident[:, :], ident[:, :])

            def bias_product():
                pe.wait_ge(w_loaded["f"], DMA)
                pe.wait_ge(bv_widened, 1)
                for k in range(KC):
                    last = nc.tensor.matmul(scores_ps[:, 0:HID], bv_wide[:, k, :], w_raw["f"][:, k, :],
                                            start=k == 0, stop=k == KC - 1)
                last.then_inc(bias_mm, 1)

            def step(i, c):
                t = TURN * i + c
                g = 2 * i + c // GROUP + 1
                first = isinstance(t, int) and t == 0
                if first:
                    past(pe, w_split["v"], KC - 1)
                    v_product(c, t)
                if real(t):
                    scores(i, c, t)
                jobs = QK_STEPS[c % GROUP] if real(g, BATCH // GROUP) else []
                if isinstance(t, int) and t in (1, 2):
                    qk_product(i, c, g, jobs[0])
                    jobs = jobs[1:]
                if real(t - 2):
                    ctx_product(c, t, t - 2)
                if real(t - 1):
                    transpose_probs(c, t - 1)
                if real(t) and in_tail(t):
                    v_product(c, t)
                for j in jobs:
                    qk_product(i, c, g, j)
                if isinstance(t, int) and t == 2 - GROUP:
                    bias_product()
                if isinstance(t, int) and t == 2:
                    past(pe, w_split["f"], KC - 1)
                if real(t - 2):
                    out_product(t, t - 2)
                if real(t) and not first and not in_tail(t):
                    v_product(c, t)
                if real(t + X_AHEAD):
                    transpose_x(i, c, t, t + X_AHEAD)
                if isinstance(t, int) and t + X_AHEAD in WARM_UPS:
                    warm_up(WARM_UPS[t + X_AHEAD])

            pe.wait_ge(ident_ready, 2)
            warm_up(WARM_UPS[-1])
            run_steps(pe, step, BATCH + 2)

        @block.vector
        def _(dve):
            def split_weight(m):
                for k in range(KC):
                    cols = slice(k * P, (k + 1) * P)
                    past(dve, w_hi_ready[m], k)
                    nc.vector.tensor_tensor(w_lo[m][:, :, cols], w_raw[m][:, :, cols],
                                            w_hi[m][:, :, cols].bitcast(F32), ALU.subtract).then_inc(w_split[m], 1)

            def split_ctx(n):
                past(dve, cT_hi_ready, n)
                nc.vector.tensor_tensor(cT_lo[:, :, :], chunks(vc_ps), cT_hi[:, :, :].bitcast(F32),
                                        ALU.subtract).then_inc(cT_split, 1)

            def split_x(i, c, n):
                par, b = x_slot(c)
                past(dve, xT_hi_ready, n)
                nc.vector.tensor_tensor(xT_lo[:, par, :, b], chunks(xT_bank(n)),
                                        xT_hi[:, par, :, b].bitcast(F32), ALU.subtract).then_inc(xT_split, 1)

            def mask_and_max(c, t):
                slot = c % 2
                past(dve, scores_done, t)
                past(dve, masked_ready, t)
                past(dve, exp_done, t - 2)
                apart(dve)
                for h in range(HEADS):
                    last = nc.vector.tensor_tensor_reduce(
                        out=s_mask[:, slot, h, :], in0=scores_ps[:, heads(h)], in1=mask_bias[:, slot, :],
                        scale=SCALE, scalar=LOWEST, op0=ALU.add, op1=ALU.max,
                        accum_out=row_max[:, slot, h:h + 1])
                last.then_inc(max_found, 1)
                past(dve, max_found, t)
                nc.vector.tensor_scalar(neg_max[:, slot, :], row_max[:, slot, :], -1.0, None, ALU.mult
                                        ).then_inc(max_negated, 1)

            def split_qk(c, g, j):
                mat, m = QK_JOBS[j]
                par = (c // GROUP + 1) % 2
                past(dve, qk_hi_ready, g * NJ + j)
                src = qk_ps[j % 2]
                if mat == "q":
                    nc.vector.scalar_tensor_tensor(
                        out=qT_lo[:, par, m, :], in0=src[:, :], scalar=bq_col[:, m:m + 1],
                        in1=qT_hi[:, par, m, :].bitcast(F32), op0=ALU.add, op1=ALU.subtract).then_inc(qk_split, 1)
                    return
                for half in range(2):
                    rows = slice(half * HEAD, (half + 1) * HEAD)
                    last = nc.vector.scalar_tensor_tensor(
                        out=kT_lo[rows, par, m, :, half, :], in0=src[rows, :].rearrange("p (b k) -> p b k", k=SEQ),
                        scalar=bk_col[rows, m:m + 1], in1=kT_hi[rows, par, m, :, half, :].bitcast(F32),
                        op0=ALU.add, op1=ALU.subtract)
                last.then_inc(qk_split, 1)

            def invert_sums(c, t):
                slot = c % 2
                past(dve, exp_done, t)
                past(dve, probs_ready, t - 2)
                nc.vector.reciprocal(inv_sum[:, slot, :], row_sum[:, slot, :]).then_inc(sum_inverted, 1)
                if isinstance(t, int) and t == BATCH - 1:
                    past(dve, sum_inverted, t)
                    past(dve, probs_ready, t - 1)
                    nc.vector.tensor_tensor(probs[:, slot, :, :], probs[:, slot, :, :],
                                            inv_sum[:, slot, :].unsqueeze(2).broadcast_to([P, HEADS, SEQ]), ALU.mult
                                            ).then_inc(probs_ready, 1)

            def residual_and_stats(i, c, n):
                slot, y = c % 2, (c - 2) % Y_RING
                past(dve, out_done, n)
                past(dve, x_biased, n)
                if isinstance(n, int):
                    if n >= Y_RING:
                        dve.wait_ge(y_stored[y], DMA * (n // Y_RING))
                else:
                    dve.wait_ge(y_stored[y], (2 * i + (c - 2) // Y_RING) * DMA)
                nc.vector.tensor_tensor(y_sb[:, y, :], ox_ps[:, 0:HID], x_bias[:, (c - 2) % X_RING, :], ALU.add
                                        ).then_inc(y_added, 1)
                past(dve, y_added, n)
                nc.vector.bn_stats(stats[:, slot, :], y_sb[:, y, :]).then_inc(y_stats, 1)
                past(dve, y_stats, n)
                past(dve, y_ready, n - 2)
                apart(dve)
                nc.vector.bn_aggr(mean_var[:, slot, :], stats[:, slot, :]).then_inc(y_aggr, 1)
                past(dve, y_aggr, n)
                nc.vector.tensor_scalar(var_eps[:, slot, :], mean_var[:, slot, 1:2], EPS, None, ALU.add
                                        ).then_inc(var_ready, 1)
                if isinstance(n, int) and n == BATCH - 1:
                    past(dve, rstd_ready, n)
                    nc.vector.tensor_scalar(y_sb[:, y, :], y_sb[:, y, :], mean_var[:, slot, 0:1],
                                            rstd[:, slot, 0:1], ALU.subtract, ALU.mult).then_inc(last_y_ready, 1)

            def step(i, c):
                t = TURN * i + c
                g = 2 * i + c // GROUP + 1
                if isinstance(t, int) and t == 1 - GROUP:
                    dve.wait_ge(biases_loaded, 4 * DMA)
                    nc.vector.tensor_copy(bv_wide[:, :, :], bv_col[:, :].unsqueeze(2).broadcast_to([P, KC, P])
                                          ).then_inc(bv_widened, 1)
                urgent = c % GROUP == 0
                if real(t + X_AHEAD - 1) and urgent:
                    split_x(i, c, t + X_AHEAD - 1)
                if isinstance(t, int) and t == -GROUP:
                    split_weight("q")
                    split_weight("k")
                if isinstance(t, int) and t == 3 - GROUP:
                    dve.wait_ge(bias_mm, 1)
                    nc.vector.tensor_tensor(bias_row[:, :], scores_ps[:, 0:HID], bf_row[:, :], ALU.add
                                            ).then_inc(bias_row_ready, 1)
                if real(t):
                    mask_and_max(c, t)
                if real(t + X_AHEAD - 1) and not urgent:
                    split_x(i, c, t + X_AHEAD - 1)
                if real(t - 2):
                    split_ctx(t - 2)
                if real(t):
                    invert_sums(c, t)
                jobs = QK_STEPS[c % GROUP] if real(g, BATCH // GROUP) else []
                if isinstance(t, int) and t == -1:
                    split_weight("f")
                before = jobs if c % GROUP == GROUP - 1 else jobs[:-1]
                for j in before:
                    split_qk(c, g, j)
                if real(t - 2):
                    residual_and_stats(i, c, t - 2)
                for j in jobs[len(before):]:
                    split_qk(c, g, j)
                if isinstance(t, int) and t == 1 - GROUP:
                    split_weight("v")

            run_steps(dve, step, BATCH + 2)

        @block.scalar
        def _(act):
            load_weight(act, "q", wq)

            def round_weight(m):
                act.wait_ge(w_loaded[m], DMA)
                for k in range(KC):
                    cols = slice(k * P, (k + 1) * P)
                    nc.scalar.copy(w_hi[m][:, :, cols], w_raw[m][:, :, cols]).then_inc(w_hi_ready[m], 1)

            def round_x(i, c, n):
                g = 2 * i + 1 + (c + 3) // GROUP
                par, b = x_slot(c)
                past(act, xT_done, n)
                past(act, qk_done, g - 2, per=NJ)
                past(act, v_done, n - TURN)
                nc.scalar.copy(xT_hi[:, par, :, b], chunks(xT_bank(n))).then_inc(xT_hi_ready, 1)

            def round_ctx(n):
                past(act, ctx_done, n)
                past(act, out_done, n - 1)
                nc.scalar.copy(cT_hi[:, :, :], chunks(vc_ps)).then_inc(cT_hi_ready, 1)

            def copy_pT(n):
                past(act, pT_done, n)
                past(act, ctx_done, n - 1)
                nc.scalar.copy(pT[:, :, :].rearrange("p h q -> p (h q)"), pT_ps[:, heads(0, HEADS)]
                               ).then_inc(pT_copied, 1)

            def exps(c, t):
                slot = c % 2
                past(act, max_negated, t)
                past(act, pT_done, t - 2)
                for h in range(HEADS):
                    last = nc.scalar.activation(probs[:, slot, h, :], s_mask[:, slot, h, :], ACT.Exp,
                                                bias=neg_max[:, slot, h:h + 1], scale=1.0,
                                                accum_out=row_sum[:, slot, h:h + 1])
                last.then_inc(exp_done, 1)

            def copy_v(c, n):
                slot = c % V_RING
                past(act, v_done, n)
                past(act, ctx_done, n - V_RING)
                nc.scalar.copy(v_sb[:, slot, :], v_bank(n)[:, 0:HID]).then_inc(v_copied, 1)

            def round_qk(c, g, j):
                mat, m = QK_JOBS[j]
                par = (c // GROUP + 1) % 2
                past(act, qk_done, g * NJ + j)
                past(act, scores_done, (g - 1) * GROUP - 1)
                src = qk_ps[j % 2]
                if mat == "q":
                    nc.scalar.activation(qT_hi[:, par, m, :], src[:, :], ACT.Identity,
                                         bias=bq_col[:, m:m + 1], scale=1.0).then_inc(qk_hi_ready, 1)
                    return
                for half in range(2):
                    rows = slice(half * HEAD, (half + 1) * HEAD)
                    last = nc.scalar.activation(kT_hi[rows, par, m, :, half, :],
                                                src[rows, :].rearrange("p (b k) -> p b k", k=SEQ), ACT.Identity,
                                                bias=bk_col[rows, m:m + 1], scale=1.0)
                last.then_inc(qk_hi_ready, 1)

            def step(i, c):
                t = TURN * i + c
                g = 2 * i + c // GROUP + 1
                if real(t + X_AHEAD - 1):
                    round_x(i, c, t + X_AHEAD - 1)
                if isinstance(t, int) and t == -GROUP:
                    round_weight("q")
                    round_weight("k")
                if real(t - 2):
                    round_ctx(t - 2)
                if real(t):
                    exps(c, t)
                if isinstance(t, int) and t == -GROUP:
                    act.wait_ge(biases_loaded, 4 * DMA)
                    act.wait_ge(k_zeroed, 2)
                jobs = QK_STEPS[c % GROUP] if real(g, BATCH // GROUP) else []
                for j in jobs[:1]:
                    round_qk(c, g, j)
                if real(t - 1):
                    copy_pT(t - 1)
                for j in jobs[1:]:
                    round_qk(c, g, j)
                if real(t):
                    copy_v(c, t)

            run_steps(act, step, BATCH + 2)

        @block.gpsimd
        def _(pool):
            nc.gpsimd.memset(minus_half[:, :], -0.5).then_inc(half_ready, 1)
            nc.gpsimd.memset(ident[:, :], 0.0).then_inc(ident_ready, 1)
            pool.wait_ge(ident_ready, 1)
            nc.gpsimd.affine_select(out=ident[:, :], in_=ident[:, :], compare_op=ALU.not_equal, fill=1.0,
                                    base=0, pattern=[[-1, P]], channel_multiplier=1).then_inc(ident_ready, 1)
            for part in (kT_hi, kT_lo):
                nc.gpsimd.memset(part[:, :, :, :, :, :].bitcast(F32), 0.0).then_inc(k_zeroed, 1)
            for m in "vf":
                pool.wait_ge(w_loaded[m], DMA)
                for k in range(KC):
                    cols = slice(k * P, (k + 1) * P)
                    nc.gpsimd.tensor_copy(w_hi[m][:, :, cols], w_raw[m][:, :, cols]).then_inc(w_hi_ready[m], 1)
            pool.wait_ge(half_ready, 1)

            def make_mask_bias(i, c, n):
                b = (c + 1) % GROUP
                par = (c + 1) // GROUP % 2
                past(pool, adj_loaded[par], i + (c + 1) // TURN, per=DMA)
                past(pool, max_found, n - 2)
                apart(pool)
                nc.gpsimd.tensor_scalar(mask_bias[:, (c + 1) % 2, :], adj_u8[:, par, b, :], -MASKED / SCALE, MASKED / SCALE,
                                        ALU.mult, ALU.add).then_inc(masked_ready, 1)

            def add_bias(i, c, n):
                slot = (c + BIAS_AHEAD) % X_RING
                past(pool, x_loaded[slot], i + (c + BIAS_AHEAD) // TURN, per=DMA)
                past(pool, y_added, n - X_RING)
                nc.gpsimd.tensor_tensor(x_bias[:, slot, :], x_in[:, slot, :], bias_row[:, :], ALU.add
                                        ).then_inc(x_biased, 1)

            def normalise_y(c, n):
                slot, y = c % 2, (c - 2) % Y_RING
                past(pool, var_ready, n)
                nc.gpsimd.tensor_tensor(rstd[:, slot, :], var_eps[:, slot, :], minus_half[:, :], ALU.pow
                                        ).then_inc(rstd_ready, 1)
                if isinstance(n, int) and n == BATCH - 1:
                    return
                past(pool, rstd_ready, n)
                apart(pool)
                nc.gpsimd.tensor_scalar(y_sb[:, y, :], y_sb[:, y, :], mean_var[:, slot, 0:1], rstd[:, slot, 0:1],
                                        ALU.subtract, ALU.mult).then_inc(y_ready, 1)

            def normalise_probs(c, t):
                slot = c % 2
                past(pool, sum_inverted, t)
                nc.gpsimd.tensor_tensor(probs[:, slot, :, :], probs[:, slot, :, :],
                                        inv_sum[:, slot, :].unsqueeze(2).broadcast_to([P, HEADS, SEQ]), ALU.mult
                                        ).then_inc(probs_ready, 1)

            def step(i, c):
                t = TURN * i + c
                if real(t + 1):
                    make_mask_bias(i, c, t + 1)
                if isinstance(t, int) and t == -BIAS_AHEAD:
                    pool.wait_ge(bias_row_ready, 1)
                if real(t + BIAS_AHEAD):
                    add_bias(i, c, t + BIAS_AHEAD)
                if real(t) and not (isinstance(t, int) and t == BATCH - 1):
                    normalise_probs(c, t)
                if real(t - 2):
                    normalise_y(c, t - 2)

            run_steps(pool, step, BATCH + 2)


_INS = ["x", "adj", "L0_gnn_Wq", "L0_gnn_bq", "L0_gnn_Wk", "L0_gnn_bk", "L0_gnn_Wv", "L0_gnn_bv",
        "L0_gnn_Wf", "L0_gnn_bf"]


def kernel(**inputs):
    import numpy as _np
    import concourse.bacc as _bacc
    from concourse import mybir as _mybir
    from concourse.bass_utils import run_bass_kernel_spmd as _run

    nc = _bacc.Bacc("TRN2", target_bir_lowering=False, num_devices=1)
    arrays, args = {}, []
    for name in _INS:
        a = _np.ascontiguousarray(inputs[name])
        arrays[f"in_{name}"] = a
        args.append(nc.dram_tensor(f"in_{name}", a.shape, _mybir.dt.from_np(a.dtype), kind="ExternalInput").ap())
    out = nc.dram_tensor("out_0", (BATCH, SEQ, HID), F32, kind="ExternalOutput").ap()
    attention_block(nc, *args, out)
    r = _run(nc, [arrays], core_ids=[0])
    return r.results[0]["out_0"]
```
